# Optimizing a Trainium2 kernel written in Bass

```python
import numpy as np
import jax
import jax.numpy as jnp

def _softmax(x, axis=-1):
    return jax.nn.softmax(x, axis=axis)

def _gelu(x):
    return jax.nn.gelu(x, approximate=True)

def _silu(x):
    return jax.nn.silu(x)

def _sigmoid(x):
    return jax.nn.sigmoid(x)

def _layernorm(x, axis=-1, eps=1e-05):
    m = jnp.mean(x, axis=axis, keepdims=True)
    v = jnp.var(x, axis=axis, keepdims=True)
    return (x - m) / jnp.sqrt(v + eps)

def _scatter_add(tgt, idx, src, axis=0):
    return tgt.at[idx].add(src)

def _segment_sum(src, seg, n):
    return jax.ops.segment_sum(src, seg, n)
kernel_name = 'mk_xattn_ffn_d2_seqx_r8_e258b0'

def setup_inputs(seed: int=0):
    np.random.seed(seed)
    _w = jnp.asarray

    def _rec_inputs():
        import jax
        import jax.numpy as jnp
        _rk = jax.random.key(seed)
        x = 7.22e-05 + 1 * jax.random.normal(jax.random.fold_in(_rk, 1), (4, 256, 256), jnp.float32)
        _lenS = 256 - jax.random.randint(jax.random.fold_in(_rk, 7), (4,), 0, max(1, 256 // 4) + 1, jnp.int32)
        _lenS2 = 256 - jax.random.randint(jax.random.fold_in(_rk, 8), (4,), 0, max(1, 256 // 4) + 1, jnp.int32)
        _ctx_1024P = jax.random.normal(jax.random.fold_in(_rk, 11), (4, 16, 128), jnp.float32)
        _ctx_1024c = jax.random.dirichlet(jax.random.fold_in(_rk, 511), 0.3 * jnp.ones((16,), jnp.float32), (4, 256))
        _ctx_1024t = jnp.einsum('bsk,bkd->bsd', _ctx_1024c, _ctx_1024P)
        _ctx_1024t = _ctx_1024t * jax.lax.rsqrt(jnp.mean(jnp.square(_ctx_1024t)) + 1e-12) * 0.953939
        ctx_1024 = 2.81802e-05 + 1.00001 * (_ctx_1024t + 0.3 * jax.random.normal(jax.random.fold_in(_rk, 611), (4, 256, 128), jnp.float32))
        fside_BxS2xS2_0 = -3.05549e-07 + 0.0199987 * jax.random.normal(jax.random.fold_in(_rk, 12), (4, 256, 256), jnp.float32)
        return (x, ctx_1024, fside_BxS2xS2_0)
    x, ctx_1024, fside_BxS2xS2_0 = _rec_inputs()

    def _L0_xattn_setup():
        import jax, jax.numpy as jnp
        import numpy as np
        key = jax.random.key(seed)
        ks = jax.random.split(key, 6)
        B, L, N, C, D = (8, 64, 256, 128, 128)
        return {'teacher_logits': jax.random.normal(ks[0], (B, L, N), dtype=jnp.float32), 'teacher_features': jax.random.normal(ks[1], (B, N, C), dtype=jnp.float32), 'Wq': jax.random.normal(ks[2], (D, C), dtype=jnp.float32) * (1.0 / np.sqrt(C)), 'bq': jnp.zeros((D,), dtype=jnp.float32), 'Wk': jax.random.normal(ks[3], (D, C), dtype=jnp.float32) * (1.0 / np.sqrt(C)), 'bk': jnp.zeros((D,), dtype=jnp.float32)}
    _L0_xattn_all = _L0_xattn_setup()
    _L0_xattn_in = {k: v for k, v in _L0_xattn_all.items() if k in ('Wq', 'bq', 'Wk', 'bk')}
    del _L0_xattn_all

    def _L0_ffn_setup():
        import jax, jax.numpy as jnp
        import numpy as np
        TURBO_BLOCK_SIZE = 64
        TURBO_MSE_BITS = 5
        QMAX = 2 ** (TURBO_MSE_BITS - 1) - 1
        SHRINKS = np.linspace(0.4, 1.0, 16)

        def mse_quant_dequant(w):
            O, I = w.shape
            wb = w.reshape(O, I // TURBO_BLOCK_SIZE, TURBO_BLOCK_SIZE)
            amax = jnp.max(jnp.abs(wb), axis=-1, keepdims=True)
            base = jnp.maximum(amax, 1e-08) / QMAX
            best_err = jnp.full(amax.shape, jnp.inf, dtype=w.dtype)
            best_scale = base
            for s in SHRINKS:
                scale = base * jnp.asarray(s, dtype=w.dtype)
                deq = jnp.clip(jnp.round(wb / scale), -QMAX, QMAX) * scale
                err = jnp.sum((deq - wb) ** 2, axis=-1, keepdims=True)
                upd = err < best_err
                best_err = jnp.where(upd, err, best_err)
                best_scale = jnp.where(upd, scale, best_scale)
            deq = jnp.clip(jnp.round(wb / best_scale), -QMAX, QMAX) * best_scale
            return deq.reshape(O, I)

        def turbo_linear(x, w):
            wq = w + jax.lax.stop_gradient(mse_quant_dequant(w) - w)
            return x @ wq.T
        key = jax.random.key(seed)
        k1, k2, k3 = jax.random.split(key, 3)
        dim, mlp_mult = (256, 4)
        hidden = mlp_mult * dim
        x = jax.random.normal(k1, (4, 256, dim), dtype=jnp.float32)
        w_fc = jax.random.normal(k2, (hidden, dim), dtype=jnp.float32) * 0.02
        w_proj = jax.random.normal(k3, (dim, hidden), dtype=jnp.float32) * 0.02
        return {'x': x, 'w_fc': w_fc, 'w_proj': w_proj}
    _L0_ffn_all = _L0_ffn_setup()
    _L0_ffn_in = {k: v for k, v in _L0_ffn_all.items() if k in ('w_fc', 'w_proj')}
    del _L0_ffn_all

    def _L1_xattn_setup():
        import jax, jax.numpy as jnp
        import numpy as np
        EPS = 1e-06
        QMAX = 127.0

        def _smooth_quant_linear(x, w):
            amax_x = jnp.max(jnp.abs(x), axis=0)
            amax_w = jnp.max(jnp.abs(w), axis=0)
            s = jnp.sqrt(jnp.maximum(amax_x, EPS) / jnp.maximum(amax_w, EPS))
            s = jnp.maximum(s, EPS)
            xs = x / s
            ws = w * s
            x_scale = jnp.maximum(jnp.max(jnp.abs(xs), axis=-1, keepdims=True), EPS) / QMAX
            w_scale = jnp.maximum(jnp.max(jnp.abs(ws), axis=-1, keepdims=True), EPS) / QMAX
            x_q = jnp.clip(jnp.round(xs / x_scale), -QMAX, QMAX)
            w_q = jnp.clip(jnp.round(ws / w_scale), -QMAX, QMAX)
            return x_q @ w_q.T * x_scale * w_scale.T

        def _expert_forward(xe, guw, dw):
            h = _smooth_quant_linear(xe, guw)
            gate, up = jnp.split(h, 2, axis=-1)
            a = jax.nn.silu(gate) * up
            return _smooth_quant_linear(a, dw)
        key = jax.random.key(seed)
        k1, k2, k3 = jax.random.split(key, 3)
        E, T, D, I = (8, 256, 256, 128)
        x = jax.random.normal(k1, (E, T, D), dtype=jnp.float32)
        gate_up_weight = jax.random.normal(k2, (E, 2 * I, D), dtype=jnp.float32) * 0.02
        down_weight = jax.random.normal(k3, (E, D, I), dtype=jnp.float32) * 0.02
        return {'x': x, 'gate_up_weight': gate_up_weight, 'down_weight': down_weight}
    _L1_xattn_all = _L1_xattn_setup()
    _L1_xattn_in = {k: v for k, v in _L1_xattn_all.items() if k in ()}
    del _L1_xattn_all

    def _L1_ffn_setup():
        import jax, jax.numpy as jnp
        import numpy as np
        B, T, D = (2, 128, 256)
        H, K, DK = (4, 8, 64)
        E = 2048
        NK = 128
        key = jax.random.key(seed)
        k1, k2, k3, k4, k5 = jax.random.split(key, 5)
        x = jax.random.normal(k1, (B, T, D), dtype=jnp.float32)
        Wq = jax.random.normal(k2, (D, 2 * H * DK), dtype=jnp.float32) * 0.02
        keys = jax.random.normal(k3, (H, NK, 2, DK), dtype=jnp.float32) * 0.02
        e_down = jax.random.normal(k4, (E, D), dtype=jnp.float32) * 0.01
        e_up = jax.random.normal(k5, (E, D), dtype=jnp.float32) * 0.01
        return {'x': x, 'Wq': Wq, 'keys': keys, 'e_down': e_down, 'e_up': e_up}
    _L1_ffn_all = _L1_ffn_setup()
    _L1_ffn_in = {k: v for k, v in _L1_ffn_all.items() if k in ('Wq', 'keys', 'e_down', 'e_up')}
    del _L1_ffn_all
    return {'x': x, 'ctx_1024': ctx_1024, 'fside_BxS2xS2_0': fside_BxS2xS2_0, 'L0_xattn_Wq': _L0_xattn_in['Wq'], 'L0_xattn_bq': _L0_xattn_in['bq'], 'L0_xattn_Wk': _L0_xattn_in['Wk'], 'L0_xattn_bk': _L0_xattn_in['bk'], 'L0_ffn_w_fc': _L0_ffn_in['w_fc'], 'L0_ffn_w_proj': _L0_ffn_in['w_proj'], 'L1_ffn_Wq': _L1_ffn_in['Wq'], 'L1_ffn_keys': _L1_ffn_in['keys'], 'L1_ffn_e_down': _L1_ffn_in['e_down'], 'L1_ffn_e_up': _L1_ffn_in['e_up']}

def reference(x, ctx_1024, fside_BxS2xS2_0, L0_xattn_Wq, L0_xattn_bq, L0_xattn_Wk, L0_xattn_bk, L0_ffn_w_fc, L0_ffn_w_proj, L1_ffn_Wq, L1_ffn_keys, L1_ffn_e_down, L1_ffn_e_up):
    import jax
    import jax.numpy as jnp

    def _L0_xattn_ref(teacher_logits, teacher_features, Wq, bq, Wk, bk):
        import jax, jax.numpy as jnp
        import numpy as np
        query = jnp.einsum('bnc,dc->bnd', teacher_features, Wq) + bq
        key = jnp.einsum('bnc,dc->bnd', teacher_features, Wk) + bk
        energy = jnp.einsum('bnd,bmd->bnm', query, key)
        attention = jax.nn.softmax(energy, axis=-1)
        x_m = jnp.einsum('bln,bmn->blm', teacher_logits, attention)
        return x_m

    def _L0_ffn_ref(x, w_fc, w_proj):
        import jax, jax.numpy as jnp
        import numpy as np
        TURBO_BLOCK_SIZE = 64
        TURBO_MSE_BITS = 5
        QMAX = 2 ** (TURBO_MSE_BITS - 1) - 1
        SHRINKS = np.linspace(0.4, 1.0, 16)

        def mse_quant_dequant(w):
            O, I = w.shape
            wb = w.reshape(O, I // TURBO_BLOCK_SIZE, TURBO_BLOCK_SIZE)
            amax = jnp.max(jnp.abs(wb), axis=-1, keepdims=True)
            base = jnp.maximum(amax, 1e-08) / QMAX
            best_err = jnp.full(amax.shape, jnp.inf, dtype=w.dtype)
            best_scale = base
            for s in SHRINKS:
                scale = base * jnp.asarray(s, dtype=w.dtype)
                deq = jnp.clip(jnp.round(wb / scale), -QMAX, QMAX) * scale
                err = jnp.sum((deq - wb) ** 2, axis=-1, keepdims=True)
                upd = err < best_err
                best_err = jnp.where(upd, err, best_err)
                best_scale = jnp.where(upd, scale, best_scale)
            deq = jnp.clip(jnp.round(wb / best_scale), -QMAX, QMAX) * best_scale
            return deq.reshape(O, I)

        def turbo_linear(x, w):
            wq = w + jax.lax.stop_gradient(mse_quant_dequant(w) - w)
            return x @ wq.T
        h = jnp.maximum(turbo_linear(x, w_fc), 0.0)
        return turbo_linear(h * h, w_proj)

    def _L1_xattn_ref(x, gate_up_weight, down_weight):
        import jax, jax.numpy as jnp
        import numpy as np
        EPS = 1e-06
        QMAX = 127.0

        def _smooth_quant_linear(x, w):
            amax_x = jnp.max(jnp.abs(x), axis=0)
            amax_w = jnp.max(jnp.abs(w), axis=0)
            s = jnp.sqrt(jnp.maximum(amax_x, EPS) / jnp.maximum(amax_w, EPS))
            s = jnp.maximum(s, EPS)
            xs = x / s
            ws = w * s
            x_scale = jnp.maximum(jnp.max(jnp.abs(xs), axis=-1, keepdims=True), EPS) / QMAX
            w_scale = jnp.maximum(jnp.max(jnp.abs(ws), axis=-1, keepdims=True), EPS) / QMAX
            x_q = jnp.clip(jnp.round(xs / x_scale), -QMAX, QMAX)
            w_q = jnp.clip(jnp.round(ws / w_scale), -QMAX, QMAX)
            return x_q @ w_q.T * x_scale * w_scale.T

        def _expert_forward(xe, guw, dw):
            h = _smooth_quant_linear(xe, guw)
            gate, up = jnp.split(h, 2, axis=-1)
            a = jax.nn.silu(gate) * up
            return _smooth_quant_linear(a, dw)
        return jax.vmap(_expert_forward)(x, gate_up_weight, down_weight)

    def _L1_ffn_ref(x, Wq, keys, e_down, e_up):
        import jax, jax.numpy as jnp
        import numpy as np
        B, T, D = (2, 128, 256)
        H, K, DK = (4, 8, 64)
        E = 2048
        NK = 128
        b, t, d = x.shape
        q = (x @ Wq).reshape(b, t, H, 2, DK)
        q1, q2 = (q[..., 0, :], q[..., 1, :])
        sim1 = jnp.einsum('bthd,hkd->bthk', q1, keys[:, :, 0, :])
        sim2 = jnp.einsum('bthd,hkd->bthk', q2, keys[:, :, 1, :])
        s1, i1 = jax.lax.top_k(sim1, K)
        s2, i2 = jax.lax.top_k(sim2, K)
        all_scores = (s1[..., :, None] + s2[..., None, :]).reshape(b, t, H, K * K)
        all_indices = (i1[..., :, None] * NK + i2[..., None, :]).reshape(b, t, H, K * K)
        final_scores, pk_idx = jax.lax.top_k(all_scores, K)
        final_indices = jnp.take_along_axis(all_indices, pk_idx, axis=-1)
        w_down = e_down[final_indices]
        w_up = e_up[final_indices]
        hidden = jnp.einsum('btd,bthkd->bthk', x, w_down)
        hidden = jax.nn.silu(hidden)
        hidden = hidden * jax.nn.relu(final_scores)
        out = jnp.einsum('bthk,bthkd->btd', hidden, w_up)
        return out
    x = x + _L0_xattn_ref(_layernorm(x, axis=-1), ctx_1024, L0_xattn_Wq, L0_xattn_bq, L0_xattn_Wk, L0_xattn_bk)
    x = x + _L0_ffn_ref(_layernorm(x, axis=-1), L0_ffn_w_fc, L0_ffn_w_proj)
    x = x + _L1_xattn_ref(_layernorm(x, axis=-1), fside_BxS2xS2_0, ctx_1024)
    x = x + _L1_ffn_ref(_layernorm(x, axis=-1), L1_ffn_Wq, L1_ffn_keys, L1_ffn_e_down, L1_ffn_e_up)
    return x

_drawn_inputs = setup_inputs


def setup_inputs(seed=0):
    import zlib

    import numpy as np

    out = dict(_drawn_inputs(seed))
    spreads = {'L0_xattn_bq': (0.0, 0.1), 'L0_xattn_bk': (0.0, 0.8)}
    factors = {'L1_ffn_Wq': 8.0, 'L1_ffn_keys': 8.0, 'L1_ffn_e_down': 8.0, 'L1_ffn_e_up': 8.0}
    for name, (base, spread) in spreads.items():
        noise = np.random.default_rng([zlib.crc32(name.encode()), seed]).standard_normal(out[name].shape)
        drawn = base * np.exp(spread * noise) if base else spread * noise
        out[name] = jnp.asarray(drawn.astype(out[name].dtype))
    for name, factor in factors.items():
        out[name] = (out[name] * factor).astype(out[name].dtype)
    return out
```

```python
from contextlib import ExitStack

import concourse.bass as bass
import numpy as np
from concourse import mybir

ALU = mybir.AluOpType
ACT = mybir.ActivationFunctionType
F32 = mybir.dt.float32
BF16 = mybir.dt.bfloat16
U32 = mybir.dt.uint32
AX = mybir.AxisListType

P = 128
MAGIC = 12582912.0
LN_EPS = 1e-5
SQ_EPS = 1e-6
SQ_MAX = 127.0
TB_BLOCK = 64
TB_MAX = 15.0
TB_FLOOR = 1e-8
SHRINKS = [float(np.float32(s)) for s in np.linspace(0.4, 1.0, 16)]
NOT_BEST = 9.0


def build(nc, x, ctx_1024, fside, wq0, bq0, wk0, bk0, w_fc, w_proj, wq1, keys, e_down, e_up, out):
    B, S, D = x.shape
    C = ctx_1024.shape[2]
    HID = w_fc.shape[0]
    H, NK, _, DK = keys.shape
    E = e_down.shape[0]
    K = 8
    NT = B * S // P
    TPB = S // P
    EROWS = E // NK
    NS = len(SHRINKS)
    CH = 1024
    NBLK = CH // TB_BLOCK
    NCH = 2 * HID * D // P // CH

    ctx = ExitStack()
    with ctx:
        def sb(name, shape, dt=F32):
            return ctx.enter_context(nc.sbuf_tensor(name, shape, dt))

        def sem(name):
            return ctx.enter_context(nc.semaphore(name))

        X = sb("X", [P, NT, D])
        CTX = sb("CTX", [P, NT, C])
        GUW = sb("GUW", [P, NT, D])
        ctxT = sb("ctxT", [P, B * S])
        XN = sb("XN", [P, NT, D])
        EU = sb("EU", [P, EROWS, D])
        EDT = sb("EDT", [P, 2, E])
        keysT = sb("keysT", [P, H, NK])
        WQ1 = sb("WQ1", [P, 2, H * 2 * DK])
        ident = sb("ident", [P, P])
        identb = sb("identb", [P, P], BF16)
        ones = sb("ones", [P, P])
        magic = sb("magic", [P, 1])
        nmagic = sb("nmagic", [P, 1])
        lneps = sb("lneps", [P, 1])
        stab = sb("stab", [P, 1, NS])
        slot16 = sb("slot16", [P, 1])
        iota8 = sb("iota8", [P, 1, K])
        stats = sb("stats", [P, NT, 6])
        mv = sb("mv", [P, NT, 2])
        rstd = sb("rstd", [P, NT])
        s_slack = sb("s_slack", [P, 1])
        bq = sb("bq", [P, 1])
        bk = sb("bk", [P, 1])

        ARENA = 33 * 1024
        arena = sb("arena", [P, ARENA])

        def cut(at, n, dt=F32):
            v = arena[:, at:at + n]
            return v if dt == F32 else v.bitcast(dt)

        KI = 1024
        W = cut(0, 4 * KI)
        W1T = cut(4 * KI, 2 * KI).rearrange("p (k o) -> p k o", k=2)
        W2T = cut(6 * KI, 2 * KI).rearrange("p (k o) -> p k o", k=HID // P)
        h2T = cut(8 * KI, 8 * KI).rearrange("p (k t) -> p k t", k=HID // P)
        xnT = cut(16 * KI, 2 * KI).rearrange("p (k t) -> p k t", k=2)
        qu = cut(18 * KI, CH)
        qy = cut(19 * KI, 2 * CH).rearrange("p (s n) -> p s n", s=2)
        qr = cut(21 * KI, CH, BF16).rearrange("p (s n) -> p s n", s=2)
        qd = cut(22 * KI, 2 * CH).rearrange("p (s n) -> p s n", s=2)
        ED = cut(24 * KI, 4 * KI).rearrange("p (e d) -> p e d", e=EROWS)
        KY = cut(28 * KI, 512).rearrange("p (h c) -> p h c", h=H)
        W0 = cut(28 * KI + 512, 512).rearrange("p (w c) -> p w c", w=4)
        hr = cut(29 * KI, 1024).rearrange("p (s n) -> p s n", s=2)
        err = cut(30 * KI, NBLK * NS).rearrange("p (b j) -> p b j", b=NBLK)
        errm = cut(30 * KI + 256, NBLK * NS).rearrange("p (b j) -> p b j", b=NBLK)
        qs = cut(30 * KI + 512, 8 * NBLK).rearrange("p (s b) -> p s b", s=8)
        qkT = cut(8 * KI, 2 * KI).rearrange("p (w t) -> p w t", w=2)
        att = cut(10 * KI, 2 * KI).rearrange("p (n m) -> p n m", n=NT)
        attT = cut(12 * KI, 2 * KI).rearrange("p (n m) -> p n m", n=NT)
        xs = cut(0, 2 * KI).rearrange("p (n d) -> p n d", n=NT)
        ws = cut(2 * KI, 2 * KI).rearrange("p (n d) -> p n d", n=NT)
        xwq = cut(4 * KI, 2 * KI, BF16).rearrange("p (b w n d) -> p b w n d", b=B, w=2, n=2)
        xwT = cut(6 * KI, 2 * KI, BF16).rearrange("p (b w k t) -> p b w k t", b=B, w=2, k=2)
        hh = cut(8 * KI, 2 * KI).rearrange("p (n o) -> p n o", n=NT)
        wsb = cut(10 * KI, 1 * KI).rearrange("p (b o) -> p b o", b=B)
        sg = cut(11 * KI, 1 * KI).rearrange("p (n i) -> p n i", n=NT)
        av = cut(12 * KI, 1 * KI).rearrange("p (n i) -> p n i", n=NT)
        a2 = cut(13 * KI, 2 * KI).rearrange("p (b w n i) -> p b w n i", b=B, w=2, n=2)
        a2q = cut(15 * KI, 1 * KI, BF16).rearrange("p (b w n i) -> p b w n i", b=B, w=2, n=2)
        a2T = cut(16 * KI, 1 * KI, BF16).rearrange("p (b w t) -> p b w t", b=B, w=2)
        dg = cut(18 * KI, 2 * KI).rearrange("p (b k r c) -> p b k r c", b=B, k=2, r=2)
        dw = cut(20 * KI, 1 * KI).rearrange("p (b k c) -> p b k c", b=B, k=2)
        yy = cut(22 * KI, 2 * KI).rearrange("p (n o) -> p n o", n=NT)
        G = cut(0, 8 * KI).rearrange("p (s e t) -> p s e t", s=2, e=EROWS)
        PR = cut(8 * KI, 4 * KI).rearrange("p (s e t) -> p s e t", s=2, e=EROWS)
        iotaJ = cut(12 * KI, 1 * KI, BF16).rearrange("p (j g) -> p j g", g=32)
        iotaI = cut(13 * KI, 2 * KI, BF16).rearrange("p (j g) -> p j g", g=32)
        oh = cut(15 * KI, 2 * KI, BF16).rearrange("p (j g) -> p j g", g=32)
        msk = cut(17 * KI, 1 * KI, BF16).rearrange("p (j g) -> p j g", g=32)
        wc = cut(18 * KI, 3 * KI, BF16).rearrange("p (c j g) -> p c j g", c=3, g=32)
        xT4 = cut(21 * KI, 1 * KI).rearrange("p (s k t) -> p s k t", s=2, k=2)
        qT4 = cut(22 * KI, 2 * KI).rearrange("p (s h t) -> p s h t", s=2, h=H)
        yo = cut(24 * KI, 512).rearrange("p (s d) -> p s d", s=2)
        eqs = cut(24 * KI + 512, 256).rearrange("p (h k j) -> p h k j", h=H, k=K)
        sums = cut(24 * KI + 768, 256).rearrange("p (h k j) -> p h k j", h=H, k=K)

        m_ws = sb("m_ws", [P, B, 2])
        m_w2 = sb("m_w2", [P, B])
        m_xs = sb("m_xs", [P, B, 2])
        sm = sb("sm", [P, B, 2, 2])
        tmpa = sb("tmpa", [P, B, 2])
        tmpb = sb("tmpb", [P, B, 2])
        rsc = sb("rsc", [P, B, 4])
        rin = sb("rin", [P, B, 4])
        m_a = sb("m_a", [P, B])
        sm2 = sb("sm2", [P, B, 2])
        t2a = sb("t2a", [P, B])
        t2b = sb("t2b", [P, B])
        rsc2 = sb("rsc2", [P, B, 4])
        rin2 = sb("rin2", [P, B, 4])
        nmax = sb("nmax", [P, NT])
        esum = sb("esum", [P, NT])
        rsum = sb("rsum", [P, NT])
        s12 = sb("s12", [P, H, 2, K])
        i12 = sb("i12", [P, H, 2, K], U32)
        i12f = sb("i12f", [P, H, 2, K])
        fin = sb("fin", [P, H, K])
        pk = sb("pk", [P, H, K], U32)
        pab = sb("pab", [P, 2, H, K], U32)
        pabf = sb("pabf", [P, 2, H, K])
        isel = sb("isel", [P, 2, H, K])
        hi = sb("hi", [P, H, K])
        coef = sb("coef", [P, H, K])
        cres = sb("cres", [P, H, K])
        pack = sb("pack", [P, 5, H * K], BF16)
        packT = sb("packT", [P, 5, H * K], BF16)

        bank = [ctx.enter_context(nc.psum_tensor(f"bank{i}", [P, 512], F32)) for i in range(8)]

        def bk2(i):
            return bank[i][:, :].rearrange("p (a n) -> p a n", a=2)

        ld = {n: sem("ld_" + n) for n in ("x", "ctx", "guw", "w0", "b0", "wfc", "wproj", "wq1", "keys", "ed", "eu")}
        s_const = sem("s_const")
        s_pool = sem("s_pool")
        s_dve = sem("s_dve")
        s_act = sem("s_act")
        names = """w0T_t w0T_e ctxT_t ctxT_e keyT_t keyT_e qk_t qk_e energy_t negmax probs_exp probs xT_t xT_e
            attT_t attT_e attn_t x1 ln1_var ln1_std ln1 guwT_t guwT_e ln2_var ln2_std ln2 x2T_t x2T_e edT_t edT_e
            scaled absolute rounded_y rounded diff squared wquant wT_t wT_e f1_t f1_e hsq f2_t x2
            ln3_var ln3_std ln3 c_xT_t c_ratio c_root c_diag c_bc_t c_pre c_quant c_qT_t c_qT_e c_h_t c_wsb c_h
            c_silu c_a c_aT_t c_ratio2 c_root2 c_diag2 c_bc2_t c_pre2 c_quant2 c_q2T_t c_q2T_e c_y_t c_wsb2 x3
            ln4_var ln4_std ln4 d_xT_t d_xT_e d_q_t d_q_e d_sim_t d_simread d_g_t d_g_e d_onehot d_c_t d_c_e
            d_up_t d_y stored0 stored1""".split()
        s = {n: sem("s_" + n) for n in names}

        block = ctx.enter_context(nc.Block())

        @block.sync
        def _(sp):
            sp.dma_start(CTX[:, :, :], ctx_1024.rearrange("b (n p) c -> p (b n) c", p=P)).then_inc(ld["ctx"], 16)
            sp.dma_start(W0[:, 0, :], wq0).then_inc(ld["w0"], 16)
            sp.dma_start(W0[:, 1, :], wk0).then_inc(ld["w0"], 16)
            sp.dma_start(bq[:, :], bq0.rearrange("(p o) -> p o", o=1)).then_inc(ld["b0"], 16)
            sp.dma_start(bk[:, :], bk0.rearrange("(p o) -> p o", o=1)).then_inc(ld["b0"], 16)
            sp.dma_start(X[:, :, :], x.rearrange("b (n p) d -> p (b n) d", p=P)).then_inc(ld["x"], 16)
            sp.dma_start(W[:, 0:2 * CH].rearrange("p (n d) -> p n d", d=D),
                         w_fc.rearrange("(n p) d -> p n d", p=P)).then_inc(ld["wfc"], 16)
            sp.dma_start(KY, keys.rearrange("h k a d -> k h (a d)")).then_inc(ld["keys"], 16)
            sp.dma_start(GUW[:, :, :], fside.rearrange("b (n p) d -> p (b n) d", p=P)).then_inc(ld["guw"], 16)
            sp.dma_start(W[:, 2 * CH:4 * CH].rearrange("p (n d) -> p n d", d=HID),
                         w_proj.rearrange("(n p) d -> p n d", p=P)).then_inc(ld["wproj"], 16)
            sp.dma_start(ED, e_down.rearrange("(n p) d -> p n d", p=P)).then_inc(ld["ed"], 16)
            sp.dma_start(WQ1[:, :, :], wq1.rearrange("(n p) c -> p n c", p=P)).then_inc(ld["wq1"], 16)
            sp.dma_start(EU[:, :, :], e_up.rearrange("(n p) d -> p n d", p=P)).then_inc(ld["eu"], 16)
            ov = out.rearrange("b (n p) d -> (b n) p d", p=P)
            for t in range(NT):
                sp.wait_ge(s["d_y"], t + 1)
                sp.dma_start(ov[t], yo[:, t % 2, :]).then_inc(s[f"stored{t % 2}"], 16)
            for i in range(2):
                sp.wait_ge(s[f"stored{i}"], 16 * (NT // 2))

        @block.gpsimd
        def _(pool):
            n = [0]

            def link(ins):
                n[0] += 1
                ins.then_inc(s_pool, 1)
                pool.wait_ge(s_pool, n[0])

            link(pool.memset(ident[:, :], 0.0))
            link(pool.affine_select(out=ident[:, :], in_=ident[:, :], compare_op=ALU.not_equal, fill=1.0, base=0,
                                    pattern=[[-1, P]], channel_multiplier=1))
            pool.tensor_copy(identb[:, :], ident[:, :])
            pool.memset(ones[:, :], 1.0)
            pool.memset(magic[:, :], MAGIC)
            pool.memset(nmagic[:, :], -MAGIC)
            pool.memset(lneps[:, :], LN_EPS)
            for j in range(NS):
                last = pool.memset(stab[:, 0, j:j + 1], SHRINKS[j])
            link(last)
            for q in range(4):
                link(pool.memset(slot16[32 * q:32 * q + 32, :], 16.0 * q))
            link(pool.iota(iota8[:, 0, :], pattern=[[1, K]], base=0, channel_multiplier=0,
                           allow_small_or_imprecise_dtypes=True))
            link(pool.memset(s_slack[:, :], 0.0))
            pool.memset(s_slack[:, :], 0.0).then_inc(s_const, 1)

            def square_hidden(i):
                m, half = i // 2, i % 2
                pool.wait_ge(s["f1_e"], i + 1)
                pool.tensor_tensor(h2T[:, m, half * 512:half * 512 + 512], hr[:, i % 2, :], hr[:, i % 2, :],
                                   ALU.mult).then_inc(s["hsq"], 1)

            for c in range(NCH):
                for j in range(NS):
                    g = c * NS + j
                    pool.wait_ge(s["rounded_y"], g + 1)
                    if g >= 2:
                        pool.wait_ge(s["diff"], g - 1)
                    pool.tensor_scalar(qr[:, j % 2, :], qy[:, j % 2, :], MAGIC + TB_MAX, MAGIC, ALU.min,
                                       ALU.subtract).then_inc(s["rounded"], 1)
                    if c in (1, 2) and 4 <= j < 12:
                        square_hidden((c - 1) * 8 + j - 4)
            pool.wait_ge(s["x3"], B)
            pool.iota(iotaJ, pattern=[[1, 64], [0, 32]], base=0, channel_multiplier=0,
                      allow_small_or_imprecise_dtypes=True)
            pool.iota(iotaI, pattern=[[1, P], [0, 32]], base=0, channel_multiplier=0,
                      allow_small_or_imprecise_dtypes=True).then_inc(s_const, 1)

        @block.tensor
        def _(pe):
            def t4(dst, src, idn, name):
                for k in range(2):
                    for n in range(2):
                        last = pe.transpose(dst[:, k, n * P:n * P + P], src[:, n, k * P:k * P + P], idn)
                return last

            pe.wait_ge(s_const, 1)
            pe.wait_ge(ld["ctx"], 16)
            for i in range(2):
                for n in range(4):
                    last = pe.transpose(bank[1 + i][:, n * P:n * P + P], CTX[:, 4 * i + n, :], ident[:, :])
                last.then_inc(s["ctxT_t"], 1)
            pe.wait_ge(ld["w0"], 32)
            for w in range(2):
                last = pe.transpose(bank[0][:, w * P:w * P + P], W0[:, w, :], ident[:, :])
            last.then_inc(s["w0T_t"], 1)
            pe.wait_ge(s["w0T_e"], 1)
            pe.wait_ge(s["ctxT_e"], 2)
            for w in range(2):
                for half in range(2):
                    pe.matmul(bank[4 + 2 * w + half][:, :], W0[:, 2 + w, :], ctxT[:, half * 512:half * 512 + 512],
                              start=True, stop=True).then_inc(s["qk_t"], 1)
            pe.wait_ge(ld["keys"], 16)
            for h in range(H):
                last = pe.transpose(bank[3][:, h * P:h * P + P], KY[:, h, :], ident[:, :])
            last.then_inc(s["keyT_t"], 1)
            pe.wait_ge(s["qk_e"], 4)
            pe.wait_ge(s["keyT_e"], 1)
            for b in range(B):
                for n in range(2):
                    at = b * S + n * P
                    last = pe.matmul(bk2(b)[:, n, :], qkT[:, 0, at:at + P], qkT[:, 1, b * S:b * S + S],
                                     start=True, stop=True)
                last.then_inc(s["energy_t"], 1)
            for b in range(B):
                pe.wait_ge(s["ln1"], b + 1)
                t4(bk2(4 + b), XN[:, 2 * b:2 * b + 2, :], ident[:, :], "").then_inc(s["xT_t"], 1)
            for b in range(B):
                pe.wait_ge(s["probs"], b + 1)
                t4(bk2(b), att[:, 2 * b:2 * b + 2, :], ident[:, :], "").then_inc(s["attT_t"], 1)
            for b in range(B):
                pe.wait_ge(s["xT_e"], b + 1)
                pe.wait_ge(s["attT_e"], b + 1)
                for n in range(2):
                    for k in range(2):
                        at = b * S + n * P
                        last = pe.matmul(bk2(4 + b)[:, n, :], xnT[:, k, at:at + P], attT[:, 2 * b + k, :],
                                         start=(k == 0), stop=(k == 1))
                last.then_inc(s["attn_t"], 1)
            pe.wait_ge(ld["guw"], 16)
            for b in range(B):
                t4(bk2(b), GUW[:, 2 * b:2 * b + 2, :], ident[:, :], "").then_inc(s["guwT_t"], 1)
            for b in range(B):
                pe.wait_ge(s["x1"], b + 1)
                pe.wait_ge(s["ln2"], b + 1)
                t4(bk2(4 + b), XN[:, 2 * b:2 * b + 2, :], ident[:, :], "").then_inc(s["x2T_t"], 1)
            pe.wait_ge(ld["ed"], 16)
            for i in range(EROWS // 2):
                if i < 4:
                    pe.wait_ge(s["guwT_e"], i + 1)
                else:
                    pe.wait_ge(s["x2T_e"], i - 3)
                t4(bk2(i), ED[:, 2 * i:2 * i + 2, :], ident[:, :], "").then_inc(s["edT_t"], 1)

            def ffn1(i):
                m, half = i // 2, i % 2
                if i < 4:
                    pe.wait_ge(s["edT_e"], 2 + i + 1)
                else:
                    pe.wait_ge(s["f1_e"], i - 3)
                for k in range(2):
                    last = pe.matmul(bank[2 + i % 4][:, :], W1T[:, k, m * P:m * P + P],
                                     xnT[:, k, half * 512:half * 512 + 512], start=(k == 0), stop=(k == 1))
                last.then_inc(s["f1_t"], 1)

            for c in range(NCH):
                pe.wait_ge(s["wquant"], c + 1)
                for i in range(2):
                    pe.wait_ge(s["edT_e"], 8)
                    if c:
                        pe.wait_ge(s["wT_e"], 2 * c - 1 + i)
                    if c < 2:
                        src = W[:, c * CH + i * 512:c * CH + i * 512 + 512].rearrange("p (n d) -> p n d", n=2)
                        t4(bk2(i), src, ident[:, :], "").then_inc(s["wT_t"], 1)
                    else:
                        for k in range(4):
                            at = c * CH + (4 * i + k) * P
                            last = pe.transpose(bank[i][:, k * P:k * P + P], W[:, at:at + P], ident[:, :])
                        last.then_inc(s["wT_t"], 1)
                if c < 2:
                    pe.wait_ge(s["wT_e"], 2 * c + 2)
                    for i in range(8):
                        ffn1(c * 8 + i)
            pe.wait_ge(s["wT_e"], 8)
            pe.wait_ge(s["hsq"], 16)
            for b in range(B):
                for n in range(2):
                    at = b * S + n * P
                    for k in range(HID // P):
                        last = pe.matmul(bk2(4 + b)[:, n, :], h2T[:, k, at:at + P], W2T[:, k, :],
                                         start=(k == 0), stop=(k == HID // P - 1))
                last.then_inc(s["f2_t"], 1)

            for b in range(B):
                pe.wait_ge(s["ln3"], b + 1)
                t4(bk2(b), XN[:, 2 * b:2 * b + 2, :], ident[:, :], "").then_inc(s["c_xT_t"], 1)
            for b in range(B):
                pe.wait_ge(s["c_diag"], b + 1)
                pe.wait_ge(s["x2"], b + 1)
                for k in range(2):
                    for r in range(2):
                        last = pe.matmul(bk2(4 + b)[:, r, k * P:k * P + P], ones[:, :], dg[:, b, k, r, :],
                                         start=True, stop=True)
                last.then_inc(s["c_bc_t"], 1)
            for b in range(B):
                pe.wait_ge(s["c_quant"], b + 1)
                qv = bank[b][:, :].bitcast(BF16).rearrange("p (w k t) -> p w k t", w=2, k=2)
                for w in range(2):
                    last = t4(qv[:, w], xwq[:, b, w], identb[:, :], "")
                last.then_inc(s["c_qT_t"], 1)
            for b in range(B):
                pe.wait_ge(s["c_qT_e"], b + 1)
                for n in range(2):
                    for k in range(2):
                        pe.matmul(bk2(b)[:, n, :], xwT[:, b, 0, k, n * P:n * P + P], xwT[:, b, 1, k, :],
                                  start=(k == 0), stop=(k == 1))
                pe.wait_ge(s["c_pre"], b + 1)
                for k in range(2):
                    last = pe.matmul(bank[4 + b][:, k * P:k * P + P], ones[:, :], dw[:, b, k, :],
                                     start=True, stop=True)
                last.then_inc(s["c_h_t"], 1)
            for b in range(B):
                pe.wait_ge(s["c_a"], b + 1)
                for n in range(2):
                    last = pe.transpose(bank[b][:, n * P:n * P + P], av[:, 2 * b + n, :], ident[:, :])
                last.then_inc(s["c_aT_t"], 1)
            for b in range(B):
                pe.wait_ge(s["c_diag2"], b + 1)
                for r in range(2):
                    last = pe.matmul(bank[4 + b][:, r * P:r * P + P], ones[:, :], dg[:, b, 0, r, :],
                                     start=True, stop=True)
                last.then_inc(s["c_bc2_t"], 1)
            for b in range(B):
                pe.wait_ge(s["c_quant2"], b + 1)
                qv = bank[b][:, 0:256].bitcast(BF16).rearrange("p (w n t) -> p w n t", w=2, n=2)
                for w in range(2):
                    for n in range(2):
                        last = pe.transpose(qv[:, w, n, :], a2q[:, b, w, n, :], identb[:, :])
                last.then_inc(s["c_q2T_t"], 1)
            for b in range(B):
                pe.wait_ge(s["c_q2T_e"], b + 1)
                for n in range(2):
                    pe.matmul(bk2(b)[:, n, :], a2T[:, b, 0, n * P:n * P + P], a2T[:, b, 1, :], start=True, stop=True)
                pe.wait_ge(s["c_pre2"], b + 1)
                for k in range(2):
                    last = pe.matmul(bank[4 + b][:, k * P:k * P + P], ones[:, :], dw[:, b, k, :],
                                     start=True, stop=True)
                last.then_inc(s["c_y_t"], 1)

            def pre(b):
                pe.wait_ge(s["ln4"], b + 1)
                if b:
                    pe.wait_ge(s["d_q_e"], 2 * b)
                t4(bk2(6), XN[:, 2 * b:2 * b + 2, :], ident[:, :], "").then_inc(s["d_xT_t"], 1)
                pe.wait_ge(s["d_xT_e"], b + 1)
                for i in range(2):
                    if i:
                        pe.wait_ge(s["d_q_e"], 2 * b + 1)
                    for h in range(2):
                        for k in range(2):
                            c0 = (2 * i + h) * P
                            last = pe.matmul(bk2(6)[:, h, :], WQ1[:, k, c0:c0 + P], xT4[:, b % 2, k, :],
                                             start=(k == 0), stop=(k == 1))
                    last.then_inc(s["d_q_t"], 1)

            def sims(b, n):
                t = 2 * b + n
                pe.wait_ge(s["d_q_e"], 2 * b + 2)
                if t:
                    pe.wait_ge(s["d_simread"], t)
                for h in range(H):
                    for a in range(2):
                        last = pe.matmul(bank[a][:, h * NK:h * NK + NK],
                                         qT4[a * DK:a * DK + DK, b % 2, h, n * P:n * P + P],
                                         keysT[a * DK:a * DK + DK, h, :], start=True, stop=True)
                last.then_inc(s["d_sim_t"], 1)

            def experts(b, lo, hi_):
                for i in range(lo, hi_):
                    g = 8 * b + i
                    if g >= 2:
                        pe.wait_ge(s["d_g_e"], g - 1)
                    for r in range(2):
                        for k in range(2):
                            at = (2 * i + r) * P
                            last = pe.matmul(bk2(4 + i % 2)[:, r, :], EDT[:, k, at:at + P], xT4[:, b % 2, k, :],
                                             start=(k == 0), stop=(k == 1))
                    last.then_inc(s["d_g_t"], 1)

            def scatter(b, n):
                t = 2 * b + n
                pe.wait_ge(s["d_onehot"], t + 1)
                for q in range(4):
                    u = 4 * t + q
                    if u >= 2:
                        pe.wait_ge(s["d_c_e"], u - 1)
                    for g8 in range(8):
                        g = 8 * q + g8
                        for c in range(3):
                            last = pe.matmul(bank[2 + q % 2][:, g8 * 64:g8 * 64 + 64], oh[:, :, g], wc[:, c, :, g],
                                             start=(c == 0), stop=(c == 2))
                    last.then_inc(s["d_c_t"], 1)

            def up(b, n):
                t = 2 * b + n
                pe.wait_ge(s["d_c_e"], 4 * t + 4)
                if t:
                    pe.wait_ge(s["d_y"], t)
                for e in range(EROWS):
                    last = pe.matmul(bk2(7)[:, n, :], PR[:, n, e, :], EU[:, e, :], start=(e == 0),
                                     stop=(e == EROWS - 1))
                last.then_inc(s["d_up_t"], 1)

            pe.wait_ge(ld["wq1"], 16)
            pe.wait_ge(ld["eu"], 16)
            pe.wait_ge(s["x3"], B)
            pre(0)
            sims(0, 0)
            experts(0, 0, 8)
            for b in range(B):
                sims(b, 1)
                scatter(b, 0)
                up(b, 0)
                if b + 1 < B:
                    pre(b + 1)
                    experts(b + 1, 0, 4)
                scatter(b, 1)
                if b + 1 < B:
                    sims(b + 1, 0)
                    experts(b + 1, 4, 8)
                up(b, 1)

        @block.scalar
        def _(act):
            act.wait_ge(s_const, 1)
            for i in range(2):
                act.wait_ge(s["ctxT_t"], i + 1)
                act.copy(ctxT[:, i * 512:i * 512 + 512], bank[1 + i][:, :]).then_inc(s["ctxT_e"], 1)
            act.wait_ge(s["w0T_t"], 1)
            act.copy(W0[:, 2:4, :], bank[0][:, 0:2 * P].rearrange("p (w c) -> p w c", w=2)).then_inc(s["w0T_e"], 1)
            act.wait_ge(ld["b0"], 32)
            for w in range(2):
                for half in range(2):
                    act.wait_ge(s["qk_t"], 2 * w + half + 1)
                    act.activation(qkT[:, w, half * 512:half * 512 + 512], bank[4 + 2 * w + half][:, :], ACT.Identity,
                                   bias=(bq, bk)[w][:, 0:1]).then_inc(s["qk_e"], 1)
            act.wait_ge(s["keyT_t"], 1)
            act.copy(keysT[:, :, :], bank[3][:, :].rearrange("p (h c) -> p h c", h=H)).then_inc(s["keyT_e"], 1)

            def std(b, n, name):
                act.wait_ge(s[name + "_var"], b + 1)
                act.activation(rstd[:, n * b:n * b + n], mv[:, n * b:n * b + n, 1], ACT.Sqrt,
                               bias=lneps[:, 0:1]).then_inc(s[name + "_std"], 1)

            std(0, NT, "ln1")
            for b in range(B):
                act.wait_ge(s["negmax"], b + 1)
                for n in range(2):
                    last = act.activation(att[:, 2 * b + n, :], bk2(b)[:, n, :], ACT.Exp,
                                          bias=nmax[:, 2 * b + n:2 * b + n + 1],
                                          accum_out=esum[:, 2 * b + n:2 * b + n + 1])
                last.then_inc(s["probs_exp"], 1)
            for b in range(B):
                act.wait_ge(s["xT_t"], b + 1)
                act.copy(xnT[:, :, b * S:b * S + S], bk2(4 + b)).then_inc(s["xT_e"], 1)
            for b in range(B):
                act.wait_ge(s["attT_t"], b + 1)
                act.copy(attT[:, 2 * b:2 * b + 2, :], bk2(b)).then_inc(s["attT_e"], 1)
            for b in range(B):
                std(b, 2, "ln2")
            for b in range(B):
                act.wait_ge(s["x2T_t"], b + 1)
                act.copy(xnT[:, :, b * S:b * S + S], bk2(4 + b)).then_inc(s["x2T_e"], 1)
            for i in range(EROWS // 2):
                act.wait_ge(s["edT_t"], i + 1)
                act.copy(EDT[:, :, i * S:i * S + S], bk2(i)).then_inc(s["edT_e"], 1)

            def weights_out(c):
                for i in range(2):
                    act.wait_ge(s["wT_t"], 2 * c + i + 1)
                    if c < 2:
                        at = c * 512 + i * 256
                        act.copy(W1T[:, :, at:at + 256], bk2(i)).then_inc(s["wT_e"], 1)
                    else:
                        act.copy(W2T[:, 4 * i:4 * i + 4, (c - 2) * P:(c - 1) * P],
                                 bank[i][:, :].rearrange("p (k o) -> p k o", k=4)).then_inc(s["wT_e"], 1)

            def relu(i):
                act.wait_ge(s["f1_t"], i + 1)
                if i >= 2:
                    act.wait_ge(s["hsq"], i - 1)
                act.activation(hr[:, i % 2, :], bank[2 + i % 4][:, :], ACT.Relu).then_inc(s["f1_e"], 1)

            for c in range(NCH):
                act.wait_ge(s["scaled"], c + 1)
                act.activation(qu, qu, ACT.Abs).then_inc(s["absolute"], 1)
                act.wait_ge(s["absolute"], c + 1)

                def shift(j):
                    g = c * NS + j
                    if g >= 2:
                        act.wait_ge(s["rounded"], g - 1)
                    act.activation(qy[:, j % 2, :], qu, ACT.Identity, bias=magic[:, 0:1],
                                   scale=float(np.float32(1.0) / np.float32(SHRINKS[j]))).then_inc(s["rounded_y"], 1)

                shift(0)
                for j in range(NS):
                    if j + 1 < NS:
                        shift(j + 1)
                    g = c * NS + j
                    act.wait_ge(s["diff"], g + 1)
                    act.activation(qd[:, j % 2, :], qd[:, j % 2, :], ACT.Square).then_inc(s["squared"], 1)
                    if c and j == 2:
                        weights_out(c - 1)
                    if c in (1, 2) and 4 <= j < 12:
                        relu((c - 1) * 8 + j - 4)
            weights_out(NCH - 1)

            for b in range(B):
                std(b, 2, "ln3")
            for b in range(B):
                act.wait_ge(s["c_ratio"], b + 1)
                act.activation(sm[:, b, 1, :], tmpa[:, b, :], ACT.Sqrt).then_inc(s["c_root"], 1)
            for b in range(B):
                act.wait_ge(s["c_pre"], b + 1)
                act.activation(xwq[:, b, 0], xs[:, 2 * b:2 * b + 2, :], ACT.Identity, bias=nmagic[:, 0:1])
                act.activation(xwq[:, b, 1], ws[:, 2 * b:2 * b + 2, :], ACT.Identity,
                               bias=nmagic[:, 0:1]).then_inc(s["c_quant"], 1)
            for b in range(B):
                act.wait_ge(s["c_qT_t"], b + 1)
                act.copy(xwT[:, b].rearrange("p w k t -> p (w k t)"), bank[b][:, :].bitcast(BF16)
                         ).then_inc(s["c_qT_e"], 1)
            for b in range(B):
                act.wait_ge(s["c_h_t"], b + 1)
                act.copy(wsb[:, b, :], bank[4 + b][:, 0:256]).then_inc(s["c_wsb"], 1)
            for b in range(B):
                act.wait_ge(s["c_h"], b + 1)
                act.activation(sg[:, 2 * b:2 * b + 2, :], hh[:, 2 * b:2 * b + 2, 0:C], ACT.Silu
                               ).then_inc(s["c_silu"], 1)
            for b in range(B):
                act.wait_ge(s["c_ratio2"], b + 1)
                act.activation(sm2[:, b, 1:2], t2a[:, b:b + 1], ACT.Sqrt).then_inc(s["c_root2"], 1)
            for b in range(B):
                act.wait_ge(s["c_pre2"], b + 1)
                act.activation(a2q[:, b].rearrange("p w n i -> p (w n i)"), a2[:, b].rearrange("p w n i -> p (w n i)"),
                               ACT.Identity, bias=nmagic[:, 0:1]).then_inc(s["c_quant2"], 1)
            for b in range(B):
                act.wait_ge(s["c_q2T_t"], b + 1)
                act.copy(a2T[:, b].rearrange("p w t -> p (w t)"), bank[b][:, 0:256].bitcast(BF16)
                         ).then_inc(s["c_q2T_e"], 1)
            for b in range(B):
                act.wait_ge(s["c_y_t"], b + 1)
                act.copy(wsb[:, b, :], bank[4 + b][:, 0:256]).then_inc(s["c_wsb2"], 1)

            for b in range(B):
                std(b, 2, "ln4")

            def queries(b):
                act.wait_ge(s["d_xT_t"], b + 1)
                act.copy(xT4[:, b % 2], bk2(6)).then_inc(s["d_xT_e"], 1)
                for i in range(2):
                    act.wait_ge(s["d_q_t"], 2 * b + i + 1)
                    act.copy(qT4[:, b % 2, 2 * i:2 * i + 2, :], bk2(6)).then_inc(s["d_q_e"], 1)

            def gate(b, lo, hi_):
                for i in range(lo, hi_):
                    g = 8 * b + i
                    act.wait_ge(s["d_g_t"], g + 1)
                    if b >= 2:
                        act.wait_ge(s["d_c_e"], 8 * (b - 1))
                    act.activation(G[:, b % 2, 2 * i:2 * i + 2, :], bk2(4 + i % 2), ACT.Silu).then_inc(s["d_g_e"], 1)

            act.wait_ge(s["x3"], B)
            queries(0)
            gate(0, 0, 8)
            for b in range(1, B):
                queries(b)
                gate(b, 0, 8)

        @block.vector
        def _(dve):
            n = [0]

            def link(ins):
                n[0] += 1
                ins.then_inc(s_dve, 1)
                dve.wait_ge(s_dve, n[0])

            def ln_stats(b, nt, name):
                for t in range(nt * b, nt * b + nt):
                    ins = dve.bn_stats(stats[:, t, :], X[:, t, :])
                link(ins)
                for t in range(nt * b, nt * b + nt):
                    ins = dve.bn_aggr(mv[:, t, :], stats[:, t, :])
                ins.then_inc(s[name + "_var"], 1)

            def ln_apply(b, nt, name):
                if nt == NT:
                    dve.wait_ge(s[name + "_std"], 1)
                else:
                    dve.wait_ge(s[name + "_std"], b + 1)
                link(dve.reciprocal(rstd[:, nt * b:nt * b + nt], rstd[:, nt * b:nt * b + nt]))
                for t in range(nt * b, nt * b + nt):
                    ins = dve.tensor_scalar(XN[:, t, :], X[:, t, :], mv[:, t, 0:1], rstd[:, t:t + 1],
                                            ALU.subtract, ALU.mult)
                    if nt == NT and t % 2:
                        ins.then_inc(s[name], 1)
                if nt != NT:
                    ins.then_inc(s[name], 1)

            dve.wait_ge(ld["x"], 16)
            dve.wait_ge(s_const, 1)
            ln_stats(0, NT, "ln1")
            ln_apply(0, NT, "ln1")
            for b in range(B):
                dve.wait_ge(s["energy_t"], b + 1)
                dve.tensor_reduce(nmax[:, 2 * b:2 * b + 2], bk2(b), AX.X, ALU.max, negate=True
                                  ).then_inc(s["negmax"], 1)
            for b in range(B):
                dve.wait_ge(s["probs_exp"], b + 1)
                link(dve.reciprocal(rsum[:, 2 * b:2 * b + 2], esum[:, 2 * b:2 * b + 2]))
                for t in (2 * b, 2 * b + 1):
                    ins = dve.tensor_scalar(att[:, t, :], att[:, t, :], rsum[:, t:t + 1], None, ALU.mult)
                ins.then_inc(s["probs"], 1)
            dve.wait_ge(s["ctxT_e"], 2)
            dve.tensor_reduce(m_w2[:, :], ctxT[:, :].rearrange("p (b t) -> p b t", b=B), AX.X, ALU.max,
                              apply_absolute_value=True)
            for b in range(B):
                dve.wait_ge(s["attn_t"], b + 1)
                xb = X[:, 2 * b:2 * b + 2, :]
                dve.tensor_tensor(xb, xb, bk2(4 + b), ALU.add).then_inc(s["x1"], 1)
            for b in range(B):
                dve.wait_ge(s["guwT_t"], b + 1)
                dve.tensor_reduce(m_ws[:, b, :], bk2(b), AX.X, ALU.max, apply_absolute_value=True
                                  ).then_inc(s["guwT_e"], 1)
            dve.wait_ge(s["x1"], B)
            for b in range(B):
                ln_stats(b, 2, "ln2")
            dve.wait_ge(s["xT_t"], B)
            for b in range(B):
                ln_apply(b, 2, "ln2")

            amax, base, rbase, errmin, best, scale, rscale = (qs[:, i, :] for i in range(7))

            def blocks(v):
                return v.rearrange("p (b n) -> p b n", n=TB_BLOCK)

            def spread(v):
                return v.unsqueeze(2).to_broadcast([P, NBLK, TB_BLOCK])

            for c in range(NCH):
                w = blocks(W[:, c * CH:c * CH + CH])
                dve.wait_ge(ld["wfc"] if c < 2 else ld["wproj"], 16)
                link(dve.tensor_reduce(amax, w, AX.X, ALU.max, apply_absolute_value=True))
                link(dve.tensor_scalar(base, amax, TB_FLOOR, float(np.float32(1.0 / TB_MAX)), ALU.max, ALU.mult))
                link(dve.reciprocal(rbase, base))
                dve.tensor_tensor(blocks(qu), w, spread(rbase), ALU.mult).then_inc(s["scaled"], 1)
                dve.wait_ge(s["scaled"], c + 1)

                def reduce_err(j):
                    dve.wait_ge(s["squared"], c * NS + j + 1)
                    return dve.tensor_reduce(err[:, :, j], blocks(qd[:, j % 2, :]), AX.X, ALU.add)

                for j in range(NS):
                    g = c * NS + j
                    dve.wait_ge(s["rounded"], g + 1)
                    dve.scalar_tensor_tensor(qd[:, j % 2, :], qr[:, j % 2, :], SHRINKS[j], qu, ALU.mult, ALU.subtract
                                             ).then_inc(s["diff"], 1)
                    if j:
                        link(reduce_err(j - 1))
                link(reduce_err(NS - 1))
                link(dve.tensor_reduce(errmin, err, AX.X, ALU.min))
                link(dve.tensor_tensor(errm, err, errmin.unsqueeze(2).to_broadcast([P, NBLK, NS]), ALU.is_gt))
                link(dve.scalar_tensor_tensor(errm, errm, NOT_BEST, stab[:, :, :].to_broadcast([P, NBLK, NS]),
                                              ALU.mult, ALU.max))
                link(dve.tensor_reduce(best, errm, AX.X, ALU.min))
                link(dve.tensor_tensor(scale, base, best, ALU.mult))
                link(dve.reciprocal(rscale, scale))
                t = blocks(qd[:, 0, :])
                link(dve.tensor_tensor(t, w, spread(rscale), ALU.mult))
                link(dve.tensor_scalar(qd[:, 0, :], qd[:, 0, :], TB_MAX, -TB_MAX, ALU.min, ALU.max))
                link(dve.tensor_scalar(qd[:, 0, :], qd[:, 0, :], MAGIC, MAGIC, ALU.add, ALU.subtract))
                link(dve.tensor_tensor(t, t, spread(scale), ALU.mult))
                link(dve.tensor_tensor(t, t, w, ALU.subtract))
                dve.tensor_tensor(w, w, t, ALU.add).then_inc(s["wquant"], 1)
                dve.wait_ge(s["wquant"], c + 1)

            for b in range(B):
                dve.wait_ge(s["f2_t"], b + 1)
                xb = X[:, 2 * b:2 * b + 2, :]
                dve.tensor_tensor(xb, xb, bk2(4 + b), ALU.add).then_inc(s["x2"], 1)
                dve.wait_ge(s["x2"], b + 1)
                ln_stats(b, 2, "ln3")
            for b in range(B):
                ln_apply(b, 2, "ln3")

            for b in range(B):
                dve.wait_ge(s["c_xT_t"], b + 1)
                link(dve.tensor_reduce(m_xs[:, b, :], bk2(b), AX.X, ALU.max, apply_absolute_value=True))
                dve.tensor_scalar(tmpa[:, b, :], m_xs[:, b, :], SQ_EPS, None, ALU.max)
                link(dve.tensor_scalar(tmpb[:, b, :], m_ws[:, b, :], SQ_EPS, None, ALU.max))
                link(dve.reciprocal(tmpb[:, b, :], tmpb[:, b, :]))
                dve.tensor_tensor(tmpa[:, b, :], tmpa[:, b, :], tmpb[:, b, :], ALU.mult).then_inc(s["c_ratio"], 1)
            for b in range(B):
                dve.wait_ge(s["c_root"], b + 1)
                link(dve.tensor_scalar(sm[:, b, 1, :], sm[:, b, 1, :], SQ_EPS, None, ALU.max))
                link(dve.reciprocal(sm[:, b, 0, :], sm[:, b, 1, :]))
                for k in range(2):
                    for r in range(2):
                        ins = dve.tensor_scalar(dg[:, b, k, r, :], ident[:, :], sm[:, b, r, k:k + 1], None, ALU.mult)
                ins.then_inc(s["c_diag"], 1)

            def row_scales(m, inv):
                link(dve.tensor_scalar(m, m, SQ_EPS, float(np.float32(1.0 / SQ_MAX)), ALU.max, ALU.mult))
                link(dve.reciprocal(inv, m))

            for b in range(B):
                dve.wait_ge(s["c_bc_t"], b + 1)
                sl = slice(2 * b, 2 * b + 2)
                dve.tensor_tensor(xs[:, sl, :], XN[:, sl, :], bk2(4 + b)[:, 0:1, :].to_broadcast([P, 2, D]), ALU.mult)
                link(dve.tensor_tensor(ws[:, sl, :], GUW[:, sl, :], bk2(4 + b)[:, 1:2, :].to_broadcast([P, 2, D]),
                                       ALU.mult))
                dve.tensor_reduce(rsc[:, b, 0:2], xs[:, sl, :], AX.X, ALU.max, apply_absolute_value=True)
                link(dve.tensor_reduce(rsc[:, b, 2:4], ws[:, sl, :], AX.X, ALU.max, apply_absolute_value=True))
                row_scales(rsc[:, b, :], rin[:, b, :])
                for w, v in enumerate((xs, ws)):
                    for i in range(2):
                        vt = v[:, 2 * b + i, :]
                        ins = dve.tensor_scalar(vt, vt, rin[:, b, 2 * w + i:2 * w + i + 1], SQ_MAX, ALU.mult, ALU.min)
                link(ins)
                for k in range(2):
                    dve.tensor_scalar(dw[:, b, k, :], ident[:, :], rsc[:, b, 2 + k:3 + k], None, ALU.mult)
                dve.tensor_scalar(xs[:, sl, :], xs[:, sl, :], -SQ_MAX, MAGIC, ALU.max, ALU.add)
                dve.tensor_scalar(ws[:, sl, :], ws[:, sl, :], -SQ_MAX, MAGIC, ALU.max, ALU.add
                                  ).then_inc(s["c_pre"], 1)
            for b in range(B):
                dve.wait_ge(s["c_wsb"], b + 1)
                for i in range(2):
                    ins = dve.scalar_tensor_tensor(hh[:, 2 * b + i, :], bk2(b)[:, i, :], rsc[:, b, i:i + 1],
                                                   wsb[:, b, :], ALU.mult, ALU.mult)
                ins.then_inc(s["c_h"], 1)
            for b in range(B):
                dve.wait_ge(s["c_silu"], b + 1)
                sl = slice(2 * b, 2 * b + 2)
                dve.tensor_tensor(av[:, sl, :], sg[:, sl, :], hh[:, sl, C:2 * C], ALU.mult).then_inc(s["c_a"], 1)
            for b in range(B):
                dve.wait_ge(s["c_aT_t"], b + 1)
                link(dve.tensor_reduce(m_a[:, b:b + 1], bank[b][:, 0:256], AX.X, ALU.max, apply_absolute_value=True))
                dve.tensor_scalar(t2a[:, b:b + 1], m_a[:, b:b + 1], SQ_EPS, None, ALU.max)
                link(dve.tensor_scalar(t2b[:, b:b + 1], m_w2[:, b:b + 1], SQ_EPS, None, ALU.max))
                link(dve.reciprocal(t2b[:, b:b + 1], t2b[:, b:b + 1]))
                dve.tensor_tensor(t2a[:, b:b + 1], t2a[:, b:b + 1], t2b[:, b:b + 1], ALU.mult
                                  ).then_inc(s["c_ratio2"], 1)
            for b in range(B):
                dve.wait_ge(s["c_root2"], b + 1)
                link(dve.tensor_scalar(sm2[:, b, 1:2], sm2[:, b, 1:2], SQ_EPS, None, ALU.max))
                link(dve.reciprocal(sm2[:, b, 0:1], sm2[:, b, 1:2]))
                for r in range(2):
                    ins = dve.tensor_scalar(dg[:, b, 0, r, :], ident[:, :], sm2[:, b, r:r + 1], None, ALU.mult)
                ins.then_inc(s["c_diag2"], 1)
            for b in range(B):
                dve.wait_ge(s["c_bc2_t"], b + 1)
                sl = slice(2 * b, 2 * b + 2)
                bc = bank[4 + b][:, 0:256].rearrange("p (r c) -> p r c", r=2)
                dve.tensor_tensor(a2[:, b, 0], av[:, sl, :], bc[:, 0:1, :].to_broadcast([P, 2, C]), ALU.mult)
                link(dve.tensor_tensor(a2[:, b, 1], CTX[:, sl, :], bc[:, 1:2, :].to_broadcast([P, 2, C]), ALU.mult))
                a4 = a2[:, b].rearrange("p w n i -> p (w n) i")
                link(dve.tensor_reduce(rsc2[:, b, :], a4, AX.X, ALU.max, apply_absolute_value=True))
                row_scales(rsc2[:, b, :], rin2[:, b, :])
                for i in range(4):
                    ins = dve.tensor_scalar(a4[:, i, :], a4[:, i, :], rin2[:, b, i:i + 1], SQ_MAX, ALU.mult, ALU.min)
                link(ins)
                for k in range(2):
                    dve.tensor_scalar(dw[:, b, k, :], ident[:, :], rsc2[:, b, 2 + k:3 + k], None, ALU.mult)
                dve.tensor_scalar(a4, a4, -SQ_MAX, MAGIC, ALU.max, ALU.add).then_inc(s["c_pre2"], 1)
            for b in range(B):
                dve.wait_ge(s["c_wsb2"], b + 1)
                for i in range(2):
                    ins = dve.scalar_tensor_tensor(yy[:, 2 * b + i, :], bk2(b)[:, i, :], rsc2[:, b, i:i + 1],
                                                   wsb[:, b, :], ALU.mult, ALU.mult)
                link(ins)
                xb = X[:, 2 * b:2 * b + 2, :]
                dve.tensor_tensor(xb, xb, yy[:, 2 * b:2 * b + 2, :], ALU.add).then_inc(s["x3"], 1)
                dve.wait_ge(s["x3"], b + 1)
                ln_stats(b, 2, "ln4")
            for b in range(B):
                ln_apply(b, 2, "ln4")

            dve.wait_ge(s_const, 2)

            def route(t):
                dve.wait_ge(s["d_sim_t"], t + 1)
                for h in range(H):
                    for a in range(2):
                        ins = dve.max(s12[:, h, a, :], bank[a][:, h * NK:h * NK + NK])
                link(ins)
                for h in range(H):
                    for a in range(2):
                        ins = dve.max_index(i12[:, h, a, :], s12[:, h, a, :], bank[a][:, h * NK:h * NK + NK])
                ins.then_inc(s["d_simread"], 1)
                link(dve.tensor_tensor(sums, s12[:, :, 0, :].unsqueeze(3).to_broadcast([P, H, K, K]),
                                       s12[:, :, 1, :].unsqueeze(2).to_broadcast([P, H, K, K]), ALU.add))
                flat = sums.rearrange("p h k j -> p h (k j)")
                for h in range(H):
                    ins = dve.max(fin[:, h, :], flat[:, h, :])
                link(ins)
                for h in range(H):
                    ins = dve.max_index(pk[:, h, :], fin[:, h, :], flat[:, h, :])
                dve.tensor_scalar(coef[:, :, :], fin[:, :, :], 0.0, None, ALU.max)
                dve.wait_ge(s["d_simread"], t + 1)
                dve.tensor_copy(i12f[:, :, :, :], i12[:, :, :, :])
                link(ins)
                dve.tensor_scalar(pab[:, 0], pk[:, :, :], 3, None, ALU.logical_shift_right)
                link(dve.tensor_scalar(pab[:, 1], pk[:, :, :], 7, None, ALU.bitwise_and))
                link(dve.tensor_copy(pabf[:, :, :, :], pab[:, :, :, :]))
                i8 = iota8[:, 0, :].unsqueeze(1).to_broadcast([P, H * K, K])
                for a in range(2):
                    e3 = eqs.rearrange("p h k j -> p (h k) j")
                    sel = pabf[:, a].rearrange("p h k -> p (h k)").unsqueeze(2).to_broadcast([P, H * K, K])
                    link(dve.tensor_tensor(e3, i8, sel, ALU.is_equal))
                    link(dve.tensor_tensor(eqs, eqs, i12f[:, :, a, :].unsqueeze(2).to_broadcast([P, H, K, K]),
                                           ALU.mult))
                    link(dve.tensor_reduce(isel[:, a], eqs, AX.X, ALU.add))
                pv = pack[:, :, :].rearrange("p f (h k) -> p f h k", h=H)
                link(dve.tensor_scalar(hi[:, :, :], isel[:, 0], float(EROWS), float(NK - 1), ALU.is_ge, ALU.mult))
                dve.tensor_tensor(pv[:, 1], isel[:, 1], hi[:, :, :], ALU.max)
                dve.tensor_scalar(pv[:, 0], isel[:, 0], float(EROWS - 1), slot16[:, 0:1], ALU.min, ALU.add)
                link(dve.tensor_copy(pv[:, 2], coef[:, :, :]))
                link(dve.tensor_tensor(cres[:, :, :], coef[:, :, :], pv[:, 2], ALU.subtract))
                link(dve.tensor_copy(pv[:, 3], cres[:, :, :]))
                link(dve.tensor_tensor(pv[:, 4], cres[:, :, :], pv[:, 3], ALU.subtract))
                link(dve.transpose(packT[:, :, :].rearrange("p f k -> p (f k)"),
                                   pack[:, :, :].rearrange("p f k -> p (f k)")))

                def over(f, cols):
                    return packT[:, f, :].unsqueeze(1).to_broadcast([P, cols, 32])

                if t:
                    dve.wait_ge(s["d_c_t"], 4 * t)
                dve.tensor_tensor(oh, iotaI, over(1, P), ALU.is_equal)
                link(dve.tensor_tensor(msk, iotaJ, over(0, 64), ALU.is_equal))
                for c in range(3):
                    ins = dve.tensor_tensor(wc[:, c], msk, over(2 + c, 64), ALU.mult)
                ins.then_inc(s["d_onehot"], 1)

            def weigh(t):
                b, i = t // 2, t % 2
                dve.wait_ge(s["d_g_e"], 8 * b + 8)
                if t >= 2:
                    dve.wait_ge(s["d_up_t"], t - 1)
                gv = G[:, b % 2, :, i * P:i * P + P].rearrange("p e (s g) -> p g s e", s=4)
                pv = PR[:, i, :, :].rearrange("p e (s g) -> p g s e", s=4)
                for q in range(4):
                    dve.wait_ge(s["d_c_t"], 4 * t + q + 1)
                    cv = bank[2 + q % 2][:, :].rearrange("p (g s e) -> p g s e", g=8, s=4)
                    dve.tensor_tensor(pv[:, 8 * q:8 * q + 8], cv, gv[:, 8 * q:8 * q + 8], ALU.mult
                                      ).then_inc(s["d_c_e"], 1)

            def result(t):
                dve.wait_ge(s["d_up_t"], t + 1)
                if t >= 2:
                    dve.wait_ge(s[f"stored{t % 2}"], 16 * (t // 2))
                dve.tensor_tensor(yo[:, t % 2, :], X[:, t, :], bk2(7)[:, t % 2, :], ALU.add).then_inc(s["d_y"], 1)

            for t in range(NT):
                route(t)
                weigh(t)
                if t:
                    result(t - 1)
            result(NT - 1)


_INS = ["x", "ctx_1024", "fside_BxS2xS2_0", "L0_xattn_Wq", "L0_xattn_bq", "L0_xattn_Wk", "L0_xattn_bk",
        "L0_ffn_w_fc", "L0_ffn_w_proj", "L1_ffn_Wq", "L1_ffn_keys", "L1_ffn_e_down", "L1_ffn_e_up"]


def kernel(**inputs):
    import numpy as _np
    import concourse.bacc as _bacc
    from concourse import mybir as _mybir
    from concourse.bass_utils import run_bass_kernel_spmd as _run

    nc = _bacc.Bacc("TRN2", target_bir_lowering=False, num_devices=1)
    arrays, args = {}, []
    for name in _INS:
        a = _np.ascontiguousarray(inputs[name])
        arrays[f"in_{name}_dram"] = a
        args.append(nc.dram_tensor(f"in_{name}_dram", a.shape, _mybir.dt.from_np(a.dtype), kind="ExternalInput").ap())
    out = nc.dram_tensor("out_dram", (4, 256, 256), _mybir.dt.float32, kind="ExternalOutput").ap()
    build(nc, *args, out)
    r = _run(nc, [arrays], core_ids=[0])
    return r.results[0]["out_dram"]
```
